# Optimizing a Trainium2 kernel written in Bass

```python
import numpy as np
import jax
import jax.numpy as jnp

def _softmax(x, axis=-1):
    return jax.nn.softmax(x, axis=axis)

def _gelu(x):
    return jax.nn.gelu(x, approximate=True)

def _silu(x):
    return jax.nn.silu(x)

def _sigmoid(x):
    return jax.nn.sigmoid(x)

def _layernorm(x, axis=-1, eps=1e-05):
    m = jnp.mean(x, axis=axis, keepdims=True)
    v = jnp.var(x, axis=axis, keepdims=True)
    return (x - m) / jnp.sqrt(v + eps)

def _scatter_add(tgt, idx, src, axis=0):
    return tgt.at[idx].add(src)

def _segment_sum(src, seg, n):
    return jax.ops.segment_sum(src, seg, n)
kernel_name = 'mk_gps_d1_gnn_r8_d618f6'

def setup_inputs(seed: int=0):
    np.random.seed(seed)
    _w = jnp.asarray

    def _rec_inputs():
        import jax
        import jax.numpy as jnp
        _gk = jax.random.key(seed)
        x = -0.0003713 + 1 * jax.random.normal(jax.random.fold_in(_gk, 1), (6250, 256), jnp.float32)
        src = jax.random.randint(jax.random.fold_in(_gk, 2), (200000,), 0, 6250, jnp.int32)
        dst = jnp.minimum((6250 * jax.random.uniform(jax.random.fold_in(_gk, 3), (200000,)) ** 2.0).astype(jnp.int32), 49999)
        _o = jnp.argsort(dst, stable=True)
        src = src[_o]
        dst = dst[_o]
        edge_weight = jax.random.uniform(jax.random.fold_in(_gk, 12), (200000,), jnp.float32, 0.0, 0.999999)
        return (x, src, dst, edge_weight)
    x, src, dst, edge_weight = _rec_inputs()

    def _L0_gnn_setup():
        import jax, jax.numpy as jnp
        import numpy as np
        N_NODES = 6250
        N_EDGES = 100000
        D_IN = 256
        D_OUT = 256
        key = jax.random.key(seed)
        ks = jax.random.split(key, 7)
        stdv = 1.0 / np.sqrt(D_OUT)
        x = jax.random.normal(ks[0], (N_NODES, D_IN), dtype=jnp.float32)
        edge_src = jax.random.randint(ks[1], (N_EDGES,), 0, N_NODES, dtype=jnp.int32)
        edge_dst = jax.random.randint(ks[2], (N_EDGES,), 0, N_NODES, dtype=jnp.int32)
        edge_weight = jax.random.uniform(ks[3], (N_EDGES,), dtype=jnp.float32)
        W_self = jax.random.uniform(ks[4], (D_IN, D_OUT), minval=-stdv, maxval=stdv, dtype=jnp.float32)
        W_neighbor = jax.random.uniform(ks[5], (D_IN, D_OUT), minval=-stdv, maxval=stdv, dtype=jnp.float32)
        bias = jax.random.uniform(ks[6], (D_OUT,), minval=-stdv, maxval=stdv, dtype=jnp.float32)
        return {'x': x, 'edge_src': edge_src, 'edge_dst': edge_dst, 'edge_weight': edge_weight, 'W_self': W_self, 'W_neighbor': W_neighbor, 'bias': bias}
    _L0_gnn_all = _L0_gnn_setup()
    _L0_gnn_in = {k: v for k, v in _L0_gnn_all.items() if k in ('W_self', 'W_neighbor', 'bias')}
    del _L0_gnn_all

    def _L0_mix_setup():
        import jax, jax.numpy as jnp
        import numpy as np
        HEADS, DIM_HEAD = (8, 64)
        EPS = 1e-05

        def instance_norm(t):
            mu = jnp.mean(t, axis=-1, keepdims=True)
            var = jnp.mean((t - mu) ** 2, axis=-1, keepdims=True)
            return (t - mu) * jax.lax.rsqrt(var + EPS)
        key = jax.random.key(seed)
        k1, k2, k3, k4 = jax.random.split(key, 4)
        B, N, D = (8, 1024, 256)
        inner = HEADS * DIM_HEAD
        x = jax.random.normal(k1, (B, N, D), jnp.float32)
        w_qkv = jax.random.normal(k2, (3 * inner, D), jnp.float32) / np.sqrt(D).astype(np.float32)
        w_out = jax.random.normal(k3, (D, inner), jnp.float32) / np.sqrt(inner).astype(np.float32)
        b_out = 0.01 * jax.random.normal(k4, (D,), jnp.float32)
        return {'x': x, 'w_qkv': w_qkv, 'w_out': w_out, 'b_out': b_out}
    _L0_mix_all = _L0_mix_setup()
    _L0_mix_in = {k: v for k, v in _L0_mix_all.items() if k in ('w_qkv', 'w_out', 'b_out')}
    del _L0_mix_all

    def _L0_ffn_setup():
        import jax, jax.numpy as jnp
        import numpy as np
        B, S, D, H, E, K = (8, 1024, 256, 1024, 8, 2)
        key = jax.random.key(seed)
        ks = jax.random.split(key, 7)
        s_in = 1.0 / np.sqrt(D)
        s_hid = 1.0 / np.sqrt(H)
        return {'x': jax.random.normal(ks[0], (B, S, D), dtype=jnp.float32), 'Wg': jax.random.uniform(ks[1], (E, D), jnp.float32, -s_in, s_in), 'bg': jax.random.uniform(ks[2], (E,), jnp.float32, -s_in, s_in), 'W1': jax.random.uniform(ks[3], (E, H, D), jnp.float32, -s_in, s_in), 'b1': jax.random.uniform(ks[4], (E, H), jnp.float32, -s_in, s_in), 'W2': jax.random.uniform(ks[5], (E, D, H), jnp.float32, -s_hid, s_hid), 'b2': jax.random.uniform(ks[6], (E, D), jnp.float32, -s_hid, s_hid)}
    _L0_ffn_all = _L0_ffn_setup()
    _L0_ffn_in = {k: v for k, v in _L0_ffn_all.items() if k in ('Wg', 'bg', 'W1', 'b1', 'W2', 'b2')}
    del _L0_ffn_all
    return {'x': x, 'src': src, 'dst': dst, 'edge_weight': edge_weight, 'L0_gnn_W_self': _L0_gnn_in['W_self'], 'L0_gnn_W_neighbor': _L0_gnn_in['W_neighbor'], 'L0_gnn_bias': _L0_gnn_in['bias'], 'L0_mix_w_qkv': _L0_mix_in['w_qkv'], 'L0_mix_w_out': _L0_mix_in['w_out'], 'L0_mix_b_out': _L0_mix_in['b_out'], 'L0_ffn_Wg': _L0_ffn_in['Wg'], 'L0_ffn_bg': _L0_ffn_in['bg'], 'L0_ffn_W1': _L0_ffn_in['W1'], 'L0_ffn_b1': _L0_ffn_in['b1'], 'L0_ffn_W2': _L0_ffn_in['W2'], 'L0_ffn_b2': _L0_ffn_in['b2']}

def reference(x, src, dst, edge_weight, L0_gnn_W_self, L0_gnn_W_neighbor, L0_gnn_bias, L0_mix_w_qkv, L0_mix_w_out, L0_mix_b_out, L0_ffn_Wg, L0_ffn_bg, L0_ffn_W1, L0_ffn_b1, L0_ffn_W2, L0_ffn_b2):
    import jax
    import jax.numpy as jnp

    def _L0_gnn_ref(x, edge_src, edge_dst, edge_weight, W_self, W_neighbor, bias):
        import jax, jax.numpy as jnp
        import numpy as np
        N_NODES = 6250
        N_EDGES = 100000
        D_IN = 256
        D_OUT = 256
        act_self = x @ W_self
        support = x @ W_neighbor
        gathered = support[edge_src] * edge_weight[:, None]
        act_neighbor = jax.ops.segment_sum(gathered, edge_dst, num_segments=N_NODES)
        return act_self + act_neighbor + bias

    def _L0_mix_ref(x, w_qkv, w_out, b_out):
        import jax, jax.numpy as jnp
        import numpy as np
        HEADS, DIM_HEAD = (8, 64)
        EPS = 1e-05

        def instance_norm(t):
            mu = jnp.mean(t, axis=-1, keepdims=True)
            var = jnp.mean((t - mu) ** 2, axis=-1, keepdims=True)
            return (t - mu) * jax.lax.rsqrt(var + EPS)
        B, N, _ = x.shape
        H, Dh = (HEADS, DIM_HEAD)
        qkv = jnp.einsum('bnd,ed->bne', x, w_qkv)
        q, k, v = jnp.split(qkv, 3, axis=-1)

        def to_heads(t):
            return t.reshape(B, N, H, Dh).transpose(0, 2, 1, 3)
        q, k, v = (to_heads(q), to_heads(k), to_heads(v))
        k = instance_norm(k)
        v = instance_norm(v)
        dots = jnp.einsum('bhnd,bhne->bhde', k, v)
        out = jnp.einsum('bhnd,bhde->bhne', q, dots) / N
        out = out.transpose(0, 2, 1, 3).reshape(B, N, H * Dh)
        return jnp.einsum('bne,de->bnd', out, w_out) + b_out

    def _L0_ffn_ref(x, Wg, bg, W1, b1, W2, b2):
        import jax, jax.numpy as jnp
        import numpy as np
        B, S, D, H, E, K = (8, 1024, 256, 1024, 8, 2)
        gate_scores = jnp.einsum('bsd,ed->bse', x, Wg) + bg
        topk_scores, topk_idx = jax.lax.top_k(gate_scores, K)
        topk_probs = jax.nn.softmax(topk_scores, axis=-1)
        combine = jnp.sum(topk_probs[..., None] * jax.nn.one_hot(topk_idx, E, dtype=x.dtype), axis=-2)
        out = jnp.zeros_like(x)
        for e in range(E):
            h = jax.nn.relu(jnp.einsum('bsd,hd->bsh', x, W1[e]) + b1[e])
            y = jnp.einsum('bsh,dh->bsd', h, W2[e]) + b2[e]
            out = out + combine[..., e:e + 1] * y
        return out
    xn = _layernorm(x, axis=-1)
    x = x + _L0_gnn_ref(xn, src, dst, edge_weight, L0_gnn_W_self, L0_gnn_W_neighbor, L0_gnn_bias) + _L0_mix_ref(xn[None], L0_mix_w_qkv, L0_mix_w_out, L0_mix_b_out)[0]
    x = x + _L0_ffn_ref(_layernorm(x, axis=-1)[None], L0_ffn_Wg, L0_ffn_bg, L0_ffn_W1, L0_ffn_b1, L0_ffn_W2, L0_ffn_b2)[0]
    return x

_drawn_inputs = setup_inputs


def setup_inputs(seed=0):
    import zlib

    import numpy as np

    out = dict(_drawn_inputs(seed))
    spreads = {}
    factors = {'L0_gnn_bias': 3.005,
     'L0_mix_b_out': 8.0,
     'L0_ffn_bg': 3.778,
     'L0_ffn_b1': 8.0,
     'L0_ffn_b2': 8.0}
    for name, (base, spread) in spreads.items():
        noise = np.random.default_rng([zlib.crc32(name.encode()), seed]).standard_normal(out[name].shape)
        drawn = base * np.exp(spread * noise) if base else spread * noise
        out[name] = jnp.asarray(drawn.astype(out[name].dtype))
    for name, factor in factors.items():
        out[name] = (out[name] * factor).astype(out[name].dtype)
    return out
```

```python
import numpy as np
import concourse.bass as bass
from concourse import mybir
from contextlib import ExitStack

F32 = mybir.dt.float32
I32 = mybir.dt.int32
ALU = mybir.AluOpType
ACT = mybir.ActivationFunctionType
AX = mybir.AxisListType

P = 128
NODES = 6250
TILES = -(-NODES // P)
ROWS = TILES * P
D = 256
KD = D // P
EDGES = 200000
GT = 8
RING = 4
GROUPS = RING * -(-EDGES // (P * GT * RING))
ECOLS = GROUPS * GT
ROUNDS = GROUPS // RING
assert ROUNDS % 2 == 1
HEADS, DH = 8, 64
INNER = HEADS * DH
PAIRS = INNER // P
E, H = 8, 1024
HJ = H // P
TOPK = 2
SLOT_TILES = 2 * -(-((ROWS * TOPK + E * (P - 1)) // P) // 2)
LEAST_TILES = ROWS * TOPK // P
EPS = 1e-5
DEEP = 4
assert TILES % 2 == TILES % DEEP == 1


def doublings(n):
    s = 1
    while s < n:
        yield s
        s *= 2


class Arena:

    def __init__(self, tensor):
        self.tensor, self.at = tensor, 0

    def take(self, *shape, dtype=F32):
        n = int(np.prod(shape))
        view = self.tensor[:, self.at:self.at + n]
        self.at += n
        if dtype != F32:
            view = view.bitcast(dtype)
        if len(shape) == 2:
            view = view.rearrange("p (a b) -> p a b", a=shape[0])
        elif len(shape) == 3:
            view = view.rearrange("p (a b c) -> p a b c", a=shape[0], b=shape[1])
        return view


class Tile:

    def __init__(self, t, s, uses):
        self.t, self.s, self.uses = t, s, uses


def over_tiles(eng, body, ring=2):
    for t in range(ring):
        body(Tile(t, t, 0))
    with eng.Fori(1, TILES // ring) as i:
        for j in range(ring):
            body(Tile(i * ring + j, j, i))
    body(Tile(TILES - 1, 0, TILES // ring))


def over_tiles_lagged(eng, head, both, tail, ring=2):
    head(Tile(0, 0, 0))
    for t in range(1, ring + 1):
        both(Tile(t, t % ring, t // ring), Tile(t - 1, t - 1, 0))
    with eng.Fori(1, TILES // ring) as i:
        for j in range(ring):
            both(Tile(i * ring + j + 1, (j + 1) % ring, i + (j + 1) // ring), Tile(i * ring + j, j, i))
    tail(Tile(TILES - 1, 0, TILES // ring))


def all_stored(eng, semaphores):
    ring = len(semaphores)
    for s, semaphore in enumerate(semaphores):
        eng.wait_ge(semaphore, 16 * (TILES // ring + (s == 0)))


def wait(eng, semaphore, value):
    if not isinstance(value, int) or value > 0:
        eng.wait_ge(semaphore, value)


class Steps:

    def __init__(self, eng, s):
        self.eng, self.s, self.n = eng, s, 0

    def __call__(self, ins):
        ins.then_inc(self.s, 1)
        self.n += 1
        self.eng.wait_ge(self.s, self.n)


def graph_layer(nc, x, src, dst, ew, w_self, w_nb, gnn_bias, w_q, w_kv, w_o, b_out, w_g, b_g, w_1, b_1, w_2, b_2, out):
    ctx = ExitStack()
    with ctx:
        def sb(name, shape, dt=F32):
            return ctx.enter_context(nc.sbuf_tensor(name, shape, dt))

        def ps(name, cols):
            return ctx.enter_context(nc.psum_tensor(name, [P, cols], F32))

        def sem(name):
            return ctx.enter_context(nc.semaphore(name))

        support_d = nc.dram_tensor("support_d", (ROWS, D), F32).ap()
        xnT_d = nc.dram_tensor("xnT_d", (TILES, P, D), F32).ap()
        x1_d = nc.dram_tensor("x1_d", (ROWS, D), F32).ap()
        xslot_d = nc.dram_tensor("xslot_d", (SLOT_TILES * P, D), F32).ap()
        yslot_d = nc.dram_tensor("yslot_d", (SLOT_TILES * P, D), F32).ap()
        rows = lambda t: t.rearrange("(t p) d -> p t d", p=P)

        ident = sb("ident", [P, P])
        iota = sb("iota", [P, P])
        ones = sb("ones", [P, P])
        before = sb("before", [P, P])
        blockno = sb("blockno", [P, TILES])
        iota8 = sb("iota8", [P, E])
        iota_i = sb("iota_i", [P, P], I32)
        epsc = sb("epsc", [P, 1])
        xn = sb("xn", [P, DEEP, D])
        xT = sb("xT", [P, 2, KD, P])
        sup = sb("sup", [P, 2, D])
        bias = sb("bias", [P, D])
        bias2 = sb("bias2", [P, D])
        st = sb("st", [P, TILES, 6])
        lnv = sb("lnv", [P, 6, TILES])
        mean, var, rstd, tmpa, tmpb, std = (lnv[:, i, :] for i in range(6))
        gtab = sb("gtab", [1, GROUPS + 1], I32)
        p1 = sb("p1", [P, TILES])
        p2 = sb("p2", [P, TILES])
        pos = sb("pos", [P, TOPK, TILES], I32)
        posx = sb("posx", [P, DEEP, TOPK], I32)
        ttab = sb("ttab", [1, 1 + SLOT_TILES], I32)
        wg = sb("wg", [P, KD, E])
        bg = sb("bg", [P, E])
        b1T = sb("b1T", [P, E * HJ])
        big = sb("big", [P, 2 * E * HJ * D])
        accs = sb("accs", [P, TILES * D])
        acc = accs[:, :].rearrange("p (t d) -> p t d", d=D)

        early = Arena(big)
        srcs = early.take(ECOLS, dtype=I32)
        dsti = early.take(ECOLS, dtype=I32)
        dloc = early.take(ECOLS)
        dblk = early.take(ECOLS)
        wts = early.take(ECOLS)
        G = early.take(RING, GT, D)
        S = early.take(GT, P)
        wkv = early.take(KD, 2 * INNER)
        wn = early.take(KD, D)
        wq = early.take(PAIRS, D)
        wo = early.take(PAIRS, D)
        ws = early.take(KD, D)
        mtot = early.take(KD, D)
        sq = early.take(2 * INNER)
        kvn = early.take(2 * INNER)
        dots = early.take(PAIRS, P)
        dwo = early.take(PAIRS, D)
        idxs = early.take(2, RING * GT, dtype=I32)
        wm = early.take(GT)
        kvs = early.take(3, 2 * HEADS)
        xk = early.take(KD, P)
        wmean = early.take(KD, 2 * HEADS)
        gmin = early.take(GROUPS)
        gmax = early.take(GROUPS)
        gcol = early.take(4)
        grow = early.take(7, GROUPS)
        zrow = early.take(7, D)
        assert early.at <= big.shape[1], early.at

        GH = GROUPS // 2

        psA = [ps(f"psA{i}", 512) for i in range(2)]
        psBB = ctx.enter_context(nc.psum_tensor("psBB", [P, 2, 512], F32))
        psB = [psBB[:, i, :] for i in range(2)]
        psC = [ps(f"psC{i}", 512) for i in range(2)]
        psD = ps("psD", 512)
        psE = ps("psE", 512)

        passed = sem("passed")

        def wait_apart(eng, *waits):
            for w, v in waits:
                wait(eng, w, v)
            if any(not isinstance(v, int) for _, v in waits):
                eng.sem_inc(passed, 1)

        def within(v, low, high):
            return nc.s_assert_within(v, low, high, skip_runtime_bounds_check_because="it follows from the tables")

        def pairs_of(eng, g):
            word = eng.value_load(gtab[0:1, bass.ds(g, 1)], min_val=0, max_val=2 ** 26 - 1)
            first = within(eng.snap(word & (2 ** 14 - 1)), 0, GROUPS * TILES)
            block0 = within(eng.snap((word >> 14) & 63), 0, TILES - 1)
            return first, block0, within(eng.snap(first + (word >> 20)), 1, GROUPS * TILES)

        def flat(v):
            return v.rearrange("p k n -> p (k n)")

        def per_head(v):
            return v.rearrange("p (h e) -> p h e", e=DH)

        def moments(step):
            me, ve, mo, vo = (st[:, :, i] for i in (1, 2, 4, 5))
            step(nc.vector.tensor_tensor(tmpa, me, mo, ALU.add))
            step(nc.vector.tensor_scalar(mean, tmpa, 0.5, None, ALU.mult))
            step(nc.vector.tensor_tensor(tmpb, me, mo, ALU.subtract))
            step(nc.vector.tensor_tensor(tmpa, tmpb, tmpb, ALU.mult))
            step(nc.vector.tensor_scalar(tmpb, tmpa, 0.25, None, ALU.mult))
            step(nc.vector.tensor_tensor(tmpa, ve, vo, ALU.add))
            step(nc.vector.scalar_tensor_tensor(out=var, in0=tmpa, scalar=1.0 / D, in1=tmpb, op0=ALU.mult, op1=ALU.add))

        x_in = [sem(f"x_in{c}") for c in range(7)]
        e_in, w_in, b_in = sem("e_in"), sem("w_in"), sem("b_in")
        k_done = sem("k_done")
        v1, v1b, v1c = sem("v1"), sem("v1b"), sem("v1c")
        stats1, std1 = sem("stats1"), sem("std1")
        rng_cols, rng_T, rng_red, rng_row = sem("rng_cols"), sem("rng_T"), sem("rng_red"), sem("rng_row")
        zeroed, xs_zero = sem("zeroed"), sem("xs_zero")
        xn_ready, xn_read, xT_ready = sem("xn_ready"), sem("xn_read"), sem("xT_ready")
        sup_mm, sup_ready = sem("sup_mm"), sem("sup_ready")
        xT_out = [sem(f"xT_out{s}") for s in range(2)]
        sup_out = [sem(f"sup_out{s}") for s in range(2)]

        with nc.Block() as block:
            @block.sync
            def _(sp):
                sp.dma_start(dsti, dst).then_inc(e_in, 16)
                for c in range(7):
                    sp.dma_start(acc[:, 7 * c:7 * c + 7, :], rows(x)[:, 7 * c:7 * c + 7, :]).then_inc(x_in[c], 16)
                sp.dma_start(wn, w_nb.rearrange("(k p) d -> p k d", p=P)).then_inc(w_in, 16)

                def store(c):
                    sp.wait_ge(xT_ready, c.t + 3)
                    sp.dma_start(xnT_d[bass.ds(c.t, 1), :, :].rearrange("a p d -> (a p) d"),
                                 flat(xT[:, c.s, :, :])).then_inc(xT_out[c.s], 16)
                    sp.wait_ge(sup_ready, c.t + 3)
                    sp.dma_start(support_d[bass.ds(c.t * P, P), :], sup[:, c.s, :]).then_inc(sup_out[c.s], 16)
                over_tiles(sp, store)
                all_stored(sp, xT_out)
                all_stored(sp, sup_out)

            @block.gpsimd
            def _(pool):
                nc.gpsimd.memset(ident[:, :], 0.0).then_inc(k_done, 1)
                nc.gpsimd.memset(before[:, :], 1.0).then_inc(k_done, 1)
                nc.gpsimd.memset(ones[:, :], 1.0).then_inc(k_done, 1)
                nc.gpsimd.memset(epsc[:, :], EPS).then_inc(k_done, 1)
                nc.gpsimd.memset(zrow, 0.0).then_inc(zeroed, 1)
                nc.gpsimd.iota(iota_i[:, :], pattern=[[1, P]], base=0, channel_multiplier=0).then_inc(k_done, 1)
                pool.wait_ge(k_done, 5)
                nc.gpsimd.affine_select(out=ident[:, :], in_=ident[:, :], compare_op=ALU.not_equal, fill=1.0,
                                        base=0, pattern=[[-1, P]], channel_multiplier=1).then_inc(k_done, 1)
                nc.gpsimd.affine_select(out=before[:, :], in_=before[:, :], compare_op=ALU.is_ge, fill=0.0,
                                        base=-1, pattern=[[1, P]], channel_multiplier=-1).then_inc(k_done, 1)
                nc.gpsimd.tensor_copy(iota[:, :], iota_i[:, :]).then_inc(k_done, 1)
                nc.gpsimd.tensor_copy(blockno[:, :], iota_i[:, 0:TILES]).then_inc(k_done, 1)
                pool.wait_ge(k_done, 9)
                nc.gpsimd.tensor_scalar(iota8[:, :], iota[:, 0:E], -float(E), None, ALU.add).then_inc(k_done, 1)
                pool.wait_ge(k_done, 10)

            @block.scalar
            def _(act):
                act.dma_start(bias[:, :], gnn_bias.partition_broadcast(P)).then_inc(b_in, 16)
                act.dma_start(bias2[:, :], b_out.partition_broadcast(P)).then_inc(b_in, 16)
                act.sem_inc(xT_ready, 2)
                act.wait_ge(k_done, 10)
                act.wait_ge(stats1, 1)
                nc.scalar.activation(std, var, ACT.Sqrt, bias=epsc[:, :], scale=1.0).then_inc(std1, 1)

                def evacuate(c):
                    wait_apart(act,
                               (xn_read, c.t + 3),
                               (xT_out[c.s], c.uses * 16),
                               (sup_mm, c.t + 1))
                    nc.scalar.activation(flat(xT[:, c.s, :, :]), psA[c.s][:, 0:D], ACT.Copy).then_inc(xT_ready, 1)

                def take_support(c):
                    wait_apart(act,
                               (sup_mm, c.t + 3),
                               (sup_out[c.s], c.uses * 16))
                    nc.scalar.activation(sup[:, c.s, :], psB[c.s][:, 0:D], ACT.Copy).then_inc(sup_ready, 1)

                def both(c, b):
                    evacuate(c)
                    take_support(b)
                act.sem_inc(sup_ready, 2)
                over_tiles_lagged(act, evacuate, both, take_support)

            @block.vector
            def _(dve):
                step = Steps(dve, v1)
                dve.wait_ge(k_done, 10)
                dve.wait_ge(e_in, 16)
                blk_i, loc_i = dblk.bitcast(I32), dloc.bitcast(I32)
                step(nc.vector.tensor_scalar(blk_i, dsti, 7, None, ALU.arith_shift_right))
                step(nc.vector.tensor_scalar(loc_i, dsti, P - 1, None, ALU.bitwise_and))
                step(nc.vector.tensor_copy(dblk, blk_i))
                step(nc.vector.tensor_copy(dloc, loc_i))
                by_group = dblk.rearrange("p (g t) -> p g t", t=GT)
                step(nc.vector.tensor_reduce(gmin, by_group, AX.X, ALU.min))
                step(nc.vector.tensor_reduce(gmax, by_group, AX.X, ALU.max))
                dve.sem_inc(rng_cols, 1)
                dve.wait_ge(rng_T, 1)
                r = psB[0][0:GH, :].rearrange("g (q p) -> g q p", q=4)
                step(nc.vector.tensor_reduce(gcol[0:GH, 0:2], r[:, 0:2, :], AX.X, ALU.min))
                step(nc.vector.tensor_reduce(gcol[0:GH, 2:4], r[:, 2:4, :], AX.X, ALU.max))
                dve.sem_inc(rng_red, 1)
                dve.wait_ge(rng_row, 1)
                lo, hi, cnt, ca, cb = (grow[0:1, i, :] for i in range(5))
                step(nc.vector.tensor_copy(lo, psB[1][0:1, 0:GROUPS]))
                step(nc.vector.tensor_copy(hi, psB[1][0:1, GROUPS:2 * GROUPS]))
                step(nc.vector.tensor_tensor(cnt, hi, lo, ALU.subtract))
                step(nc.vector.tensor_scalar(cnt, cnt, 1.0, None, ALU.add))
                step(nc.vector.tensor_copy(ca, cnt))
                for d in doublings(GROUPS):
                    step(nc.vector.tensor_copy(cb[:, 0:d], ca[:, 0:d]))
                    step(nc.vector.tensor_tensor(cb[:, d:], ca[:, d:], ca[:, 0:GROUPS - d], ALU.add))
                    ca, cb = cb, ca
                gi, gw = (grow[0:1, 5 + j, :].bitcast(I32) for j in range(2))
                step(nc.vector.tensor_copy(gtab[0:1, GROUPS:], ca[:, GROUPS - 1:]))
                step(nc.vector.tensor_copy(gi, cnt))
                step(nc.vector.tensor_scalar(gw, gi, 20, None, ALU.logical_shift_left))
                step(nc.vector.tensor_copy(gi, lo))
                step(nc.vector.tensor_scalar(gi, gi, 14, None, ALU.logical_shift_left))
                step(nc.vector.tensor_tensor(gw, gw, gi, ALU.bitwise_or))
                step(nc.vector.tensor_tensor(cb, ca, cnt, ALU.subtract))
                step(nc.vector.tensor_copy(gi, cb))
                step(nc.vector.tensor_tensor(gtab[0:1, 0:GROUPS], gw, gi, ALU.bitwise_or))
                dve.wait_ge(b_in, 32)
                step(nc.vector.tensor_tensor(bias[:, :], bias[:, :], bias2[:, :], ALU.add))
                for c in range(7):
                    dve.wait_ge(x_in[c], 16)
                    for t in range(7 * c, 7 * c + 7):
                        nc.vector.bn_stats(st[:, t, :], acc[:, t, :]).then_inc(v1b, 1)
                dve.wait_ge(v1b, TILES)
                moments(step)
                dve.sem_inc(stats1, 1)
                dve.wait_ge(std1, 1)
                step(nc.vector.reciprocal(rstd, std))
                dve.wait_ge(w_in, 16)

                def norm(c):
                    dve.wait_ge(xn_read, c.t + 1)
                    nc.vector.tensor_scalar(xn[:, c.s, :], acc[:, c.t, :], mean[:, bass.ds(c.t, 1)],
                                            rstd[:, bass.ds(c.t, 1)], ALU.subtract, ALU.mult).then_inc(xn_ready, 1)
                    nc.vector.tensor_tensor(acc[:, c.t, :], acc[:, c.t, :], bias[:, :], ALU.add).then_inc(v1c, 1)

                over_tiles(dve, norm)

            @block.tensor
            def _(pe):
                pe.wait_ge(k_done, 10)
                pe.sem_inc(xn_read, 2)
                pe.sem_inc(sup_mm, 2)
                pe.wait_ge(rng_cols, 1)
                for q, v in enumerate((gmin, gmin, gmax, gmax)):
                    half = v[:, (q % 2) * GH:(q % 2 + 1) * GH]
                    last = nc.tensor.transpose(psB[0][0:GH, q * P:(q + 1) * P], half, ident[:, :])
                last.then_inc(rng_T, 1)
                pe.wait_ge(rng_red, 1)
                for q in range(4):
                    last = nc.tensor.matmul(psB[1][0:1, q * GH:(q + 1) * GH], gcol[0:GH, q:q + 1],
                                            ident[0:GH, 0:GH], start=True, stop=True)
                last.then_inc(rng_row, 1)
                pe.wait_ge(w_in, 16)

                def turn(c):
                    pe.wait_ge(xn_ready, c.t + 1)
                    pe.wait_ge(xT_ready, c.t + 1)
                    for k in range(KD):
                        last = nc.tensor.transpose(psA[c.s][:, k * P:(k + 1) * P], xn[:, c.s, k * P:(k + 1) * P],
                                                   ident[:, :])
                    last.then_inc(xn_read, 1)

                def support(c):
                    pe.wait_ge(xT_ready, c.t + 3)
                    pe.wait_ge(sup_ready, c.t + 1)
                    for k in range(KD):
                        last = nc.tensor.matmul(psB[c.s][:, 0:D], xT[:, c.s, k, :], wn[:, k, :],
                                                start=(k == 0), stop=(k == KD - 1))
                    last.then_inc(sup_mm, 1)

                def both(c, b):
                    turn(c)
                    support(b)
                over_tiles_lagged(pe, turn, both, support)

        ed_in, kw_in, xk_in = sem("ed_in"), sem("kw_in"), sem("xk_in")
        idx_ready = sem("idx_ready")
        gathered = [sem(f"gathered{s}") for s in range(RING)]
        group_used = sem("group_used")
        v2, v2k, wm_ready, s_ready, s_used, ps_free = (sem(n) for n in (
            "v2", "v2k", "wm_ready", "s_ready", "s_used", "ps_free"))
        kv_w, kv_mm, kv_sq, kv_std, kvn_ready, dots_mm, dots_added = (sem(n) for n in (
            "kv_w", "kv_mm", "kv_sq", "kv_std", "kvn_ready", "dots_mm", "dots_added"))

        with nc.Block() as block:
            @block.sync
            def _(sp):
                sp.dma_start(srcs, src).then_inc(ed_in, 16)
                sp.dma_start(wts, ew).then_inc(ed_in, 16)
                sp.dma_start(wkv, w_kv.rearrange("(k p) d -> p k d", p=P)).then_inc(kw_in, 16)
                sp.wait_ge(zeroed, 1)
                xz = rows(xslot_d)
                zs = list(range(0, SLOT_TILES, 7))
                for z in zs:
                    n = min(7, SLOT_TILES - z)
                    sp.dma_start(xz[:, z:z + n, :], zrow[:, 0:n, :]).then_inc(xs_zero, 16)
                for z in range(LEAST_TILES, SLOT_TILES, 7):
                    n = min(7, SLOT_TILES - z)
                    sp.dma_start(rows(yslot_d)[:, z:z + n, :], zrow[:, 0:n, :]).then_inc(xs_zero, 16)
                    zs.append(z)
                with sp.Fori(0, TILES) as i:
                    sp.wait_ge(kv_mm, i + 1)
                    sp.dma_start(flat(xk), xnT_d[bass.ds(i, 1), :, :].rearrange("a p d -> (a p) d")).then_inc(xk_in, 16)
                sp.wait_ge(xk_in, 16 * TILES)
                sp.wait_ge(xs_zero, 16 * len(zs))

            @block.gpsimd
            def _(pool):
                pool.wait_ge(ed_in, 32)

                def take_sources(i, h):
                    nc.gpsimd.tensor_copy(idxs[:, h, :], srcs[:, bass.ds(i * (RING * GT), RING * GT)]).then_inc(idx_ready, 1)

                def gather_round(i, h, more=True):
                    wait_apart(pool, (idx_ready, i + 1))
                    for s in range(RING):
                        wait_apart(pool, (group_used, i * RING + s + 1))
                        if s == RING - 1 and more:
                            take_sources(i + 1, 1 - h)
                        for t in range(GT):
                            nc.gpsimd.indirect_dma_start(
                                out=G[:, s, t, :], out_offset=None, in_=support_d,
                                in_offset=bass.IndirectOffsetOnAxis(ap=idxs[:, h, s * GT + t:s * GT + t + 1], axis=0),
                            ).then_inc(gathered[s], 16)

                take_sources(0, 0)
                gather_round(0, 0)
                with pool.Fori(0, ROUNDS // 2 - 1) as j:
                    gather_round(j * 2 + 1, 1)
                    gather_round(j * 2 + 2, 0)
                gather_round(ROUNDS - 2, 1)
                gather_round(ROUNDS - 1, 0, more=False)

            @block.scalar
            def _(act):
                with act.Fori(0, TILES) as i:
                    wait_apart(act,
                               (kv_mm, i + 2),
                               (v2k, i * 2 + 1))
                    for c in range(2):
                        nc.scalar.activation(sq[:, c * INNER:(c + 1) * INNER], psA[c][:, :], ACT.Square).then_inc(kv_sq, 1)
                    act.wait_ge(v2k, i * 2 + 2)
                    nc.scalar.activation(kvs[:, 1, :], kvs[:, 0, :], ACT.Sqrt, bias=epsc[:, :],
                                         scale=1.0 / DH).then_inc(kv_std, 1)

            @block.vector
            def _(dve):
                step = Steps(dve, v2)
                dve.sem_inc(group_used, RING - 1)
                dve.sem_inc(s_used, GT)
                for free in (s_ready, ps_free, v2k, dots_added, kvn_ready):
                    dve.sem_inc(free, 1)
                dve.wait_ge(kw_in, 16)
                for k in range(KD):
                    w = per_head(wkv[:, k, :])
                    step(nc.vector.tensor_reduce(wmean[:, k, :], w, AX.X, ALU.add))
                    step(nc.vector.tensor_scalar(wmean[:, k, :], wmean[:, k, :], 1.0 / DH, None, ALU.mult))
                    step(nc.vector.tensor_tensor(w, w, wmean[:, k, :].unsqueeze(2).to_broadcast([P, 2 * HEADS, DH]),
                                                 ALU.subtract))
                step(nc.vector.memset(dots, 0.0))
                step(nc.vector.memset(psBB[:, 1, 0:D], 0.0))
                dve.sem_inc(kv_w, 1)
                dve.wait_ge(ed_in, 32)

                block_before = dve.alloc_register("block_before")
                dve.reg_mov(block_before, 0)

                def add_sum(n1):
                    b = within(dve.snap(block_before), 0, TILES - 1)
                    dve.wait_ge(ps_free, n1)
                    nc.vector.tensor_tensor(acc[:, b, :], acc[:, b, :], psBB[:, within(dve.snap(n1 & 1), 0, 1), 0:D],
                                            ALU.add).then_inc(ps_free, 1)

                def group(i, s):
                    g = i * RING + s
                    first, block0, end = pairs_of(dve, g)
                    cols = bass.ds(g * GT, GT)
                    with dve.Fori(first, end) as n:
                        b = within(dve.snap(n - first + block0), 0, TILES - 1)
                        dve.wait_ge(s_ready, n * GT + 1)
                        nc.vector.scalar_tensor_tensor(
                            out=wm, in0=dblk[:, cols], scalar=blockno[:, bass.ds(b, 1)],
                            in1=wts[:, cols], op0=ALU.is_equal, op1=ALU.mult).then_inc(wm_ready, 1)
                        dve.wait_ge(wm_ready, n + 1)
                        for t in range(GT):
                            dve.wait_ge(s_used, n * GT + t + 1)
                            nc.vector.tensor_scalar(
                                S[:, t, :], iota[:, :], dloc[:, bass.ds(g * GT + t, 1)], wm[:, t:t + 1],
                                ALU.is_equal, ALU.mult).then_inc(s_ready, 1)
                        add_sum(n + 1)
                        dve.reg_mov(block_before, b)
                    dve.sem_inc(group_used, 1)

                with dve.Fori(0, GROUPS // RING) as i:
                    group(i, 0)
                    dve.wait_ge(kv_sq, i * 2 + 2)
                    nc.vector.tensor_reduce(kvs[:, 0, :], per_head(sq), AX.X, ALU.add).then_inc(v2k, 1)
                    group(i, 1)
                    dve.wait_ge(kv_std, i + 1)
                    nc.vector.reciprocal(kvs[:, 2, :], kvs[:, 1, :]).then_inc(v2k, 1)
                    dve.wait_ge(v2k, i * 2 + 3)
                    dve.wait_ge(dots_mm, i + 1)
                    for c in range(2):
                        nc.vector.tensor_tensor(
                            per_head(kvn[:, c * INNER:(c + 1) * INNER]), per_head(psA[c][:, :]),
                            kvs[:, 2, c * HEADS:(c + 1) * HEADS].unsqueeze(2).to_broadcast([P, HEADS, DH]),
                            ALU.mult).then_inc(kvn_ready, 1)
                    group(i, 2)
                    group(i, 3)
                    dve.wait_ge(dots_mm, i + 2)
                    dve.wait_ge(dots_added, i + 1)
                    nc.vector.tensor_tensor(flat(dots), flat(dots), psC[0][:, :], ALU.add).then_inc(dots_added, 1)
                pairs = dve.value_load(gtab[0:1, GROUPS:], min_val=GROUPS, max_val=GROUPS * TILES)
                dve.wait_ge(s_used, pairs * GT + GT)
                add_sum(pairs + 1)

            @block.tensor
            def _(pe):
                pe.sem_inc(kv_mm, 1)
                pe.sem_inc(dots_mm, 1)
                pe.wait_ge(kv_w, 1)

                def group(i, s):
                    g = i * RING + s
                    first, block0, end = pairs_of(pe, g)
                    wait_apart(pe, (gathered[s], i * (16 * GT) + 16 * GT))
                    with pe.Fori(first, end) as n:
                        pe.wait_ge(ps_free, n + 1)
                        bank = within(pe.snap(n & 1), 0, 1)
                        for t in range(GT):
                            pe.wait_ge(s_ready, n * GT + t + 2)
                            nc.tensor.matmul(psBB[:, bank, 0:D], S[:, t, :], G[:, s, t, :],
                                             start=(t == 0), stop=(t == GT - 1)).then_inc(s_used, 1)

                with pe.Fori(0, GROUPS // RING) as i:
                    pe.wait_ge(xk_in, i * 16 + 16)
                    pe.wait_ge(kvn_ready, i * 2 + 1)
                    for c in range(2):
                        for k in range(KD):
                            last = nc.tensor.matmul(psA[c][:, :], xk[:, k, :], wkv[:, k, c * INNER:(c + 1) * INNER],
                                                    start=(k == 0), stop=(k == KD - 1))
                    last.then_inc(kv_mm, 1)
                    group(i, 0)
                    group(i, 1)
                    group(i, 2)
                    pe.wait_ge(kvn_ready, i * 2 + 3)
                    pe.wait_ge(dots_added, i + 1)
                    for h in range(PAIRS):
                        cols = slice(h * P, (h + 1) * P)
                        last = nc.tensor.matmul(psC[0][:, cols], kvn[:, INNER + h * P:INNER + (h + 1) * P],
                                                kvn[:, cols], start=True, stop=True)
                    last.then_inc(dots_mm, 1)
                    group(i, 3)

        m_in, masked, dwo_mm, dwo_ready, m_mm, m_ready = (sem(n) for n in (
            "m_in", "masked", "dwo_mm", "dwo_ready", "m_mm", "m_ready"))
        v3, v3b, v3c = sem("v3"), sem("v3b"), sem("v3c")
        xl_in = [sem(f"xl_in{s}") for s in range(2)]
        x1_mm, x1_add = sem("x1_mm"), sem("x1_add")
        stats3, std3, x1_out = sem("stats3"), sem("std3"), sem("x1_out")
        xn3_ready, xn3_read, xT3_ready, gate_mm = (sem(n) for n in ("xn3_ready", "xn3_read", "xT3_ready", "gate_mm"))
        gap, gap_exp, chosen, counted = (sem(n) for n in ("gap", "gap_exp", "chosen", "counted"))

        route = Arena(big)
        route.at = 5 * ECOLS
        TE = (TILES, E)
        lg, eq, cand, one1, one2, lg2, both_, ta, tb, exc, slot = (route.take(*TE) for _ in range(11))
        m1, m2, i1, gapv, gexp, den = (route.take(TILES) for _ in range(6))
        te, tc, td, base = (route.take(E) for _ in range(4))
        te_i = route.take(E, dtype=I32)
        trow = route.take(2, SLOT_TILES)
        nt_i = route.take(4, dtype=I32)
        posf = route.take(TILES)
        assert route.at <= 5 * ECOLS + RING * GT * D

        with nc.Block() as block:
            @block.sync
            def _(sp):
                sp.dma_start(wo, w_o.rearrange("(k p) d -> p k d", p=P)).then_inc(m_in, 16)
                sp.dma_start(wq, w_q.rearrange("(k p) d -> p k d", p=P)).then_inc(m_in, 16)
                sp.dma_start(ws, w_self.rearrange("(k p) d -> p k d", p=P)).then_inc(m_in, 16)
                sp.dma_start(wg[:, :, :], w_g.rearrange("(k p) e -> p k e", p=P)).then_inc(m_in, 16)
                sp.dma_start(bg[:, :], b_g.partition_broadcast(P)).then_inc(m_in, 16)
                sp.dma_start(b1T[:, :], b_1).then_inc(m_in, 16)

                def load(c):
                    sp.wait_ge(x1_mm, c.t + 1)
                    sp.dma_start(flat(xT[:, c.s, :, :]),
                                 xnT_d[bass.ds(c.t, 1), :, :].rearrange("a p d -> (a p) d")).then_inc(xl_in[c.s], 16)
                over_tiles(sp, load)
                sp.wait_ge(stats3, 1)
                for c in range(7):
                    sp.dma_start(rows(x1_d)[:, 7 * c:7 * c + 7, :], acc[:, 7 * c:7 * c + 7, :]).then_inc(x1_out, 16)
                sp.wait_ge(x1_out, 16 * 7)

            @block.scalar
            def _(act):
                act.sem_inc(xT3_ready, 2)
                act.wait_ge(stats3, 1)
                nc.scalar.activation(std, var, ACT.Sqrt, bias=epsc[:, :], scale=1.0).then_inc(std3, 1)

                def evacuate(c):
                    wait_apart(act,
                               (xn3_read, c.t + 3),
                               (gate_mm, c.t + 1))
                    nc.scalar.activation(flat(xT[:, c.s, :, :]), psA[c.s][:, 0:D], ACT.Copy).then_inc(xT3_ready, 1)
                over_tiles(act, evacuate)
                act.wait_ge(gap, 1)
                nc.scalar.activation(gexp, gapv, ACT.Exp).then_inc(gap_exp, 1)

            @block.vector
            def _(dve):
                step = Steps(dve, v3)
                step(nc.vector.memset(dots[0:DH, :, DH:P], 0.0))
                step(nc.vector.memset(dots[DH:P, :, 0:DH], 0.0))
                dve.sem_inc(masked, 1)
                dve.wait_ge(dwo_mm, 1)
                for i in range(2):
                    step(nc.vector.tensor_copy(flat(dwo[:, 2 * i:2 * i + 2, :]), psA[i][:, :]))
                dve.sem_inc(dwo_ready, 1)
                dve.wait_ge(m_mm, 1)
                dve.wait_ge(m_in, 96)
                for c in range(KD):
                    step(nc.vector.scalar_tensor_tensor(out=mtot[:, c, :], in0=psB[c][:, 0:D], scalar=1.0 / NODES,
                                                        in1=ws[:, c, :], op0=ALU.mult, op1=ALU.add))
                dve.sem_inc(m_ready, 1)

                def add(c):
                    dve.wait_ge(x1_mm, c.t + 3)
                    nc.vector.tensor_tensor(acc[:, c.t, :], acc[:, c.t, :], psC[c.s][:, 0:D], ALU.add).then_inc(x1_add, 1)

                def stats(c):
                    wait_apart(dve, (x1_add, c.t + 3))
                    nc.vector.bn_stats(st[:, c.t, :], acc[:, c.t, :]).then_inc(v3b, 1)

                def both(c, b):
                    add(c)
                    stats(b)
                dve.sem_inc(x1_add, 2)
                over_tiles_lagged(dve, add, both, stats)
                dve.wait_ge(v3b, TILES)
                moments(step)
                dve.sem_inc(stats3, 1)
                dve.wait_ge(std3, 1)
                step(nc.vector.reciprocal(rstd, std))

                def norm(c):
                    dve.wait_ge(xn3_read, c.t + 1)
                    nc.vector.tensor_scalar(xn[:, c.s, :], acc[:, c.t, :], mean[:, bass.ds(c.t, 1)],
                                            rstd[:, bass.ds(c.t, 1)], ALU.subtract, ALU.mult).then_inc(xn3_ready, 1)
                over_tiles(dve, norm)
                dve.wait_ge(gate_mm, TILES + 2)

                def by_expert(v):
                    return v.unsqueeze(1).to_broadcast([P, *TE])

                def by_tile(v):
                    return v.unsqueeze(2).to_broadcast([P, *TE])
                step(nc.vector.tensor_tensor(lg, psE[:, 0:TILES * E].rearrange("p (t e) -> p t e", e=E),
                                             by_expert(bg[:, :]), ALU.add))
                for scores, m, one in ((lg, m1, one1), (lg2, m2, one2)):
                    step(nc.vector.tensor_reduce(m, scores, AX.X, ALU.max))
                    step(nc.vector.tensor_tensor(eq, scores, by_tile(m), ALU.is_equal))
                    step(nc.vector.tensor_tensor(cand, eq, by_expert(iota8[:, :]), ALU.mult))
                    step(nc.vector.tensor_reduce(i1, cand, AX.X, ALU.min))
                    step(nc.vector.tensor_tensor(one, by_expert(iota8[:, :]), by_tile(i1), ALU.is_equal))
                    if one is one1:
                        step(nc.vector.scalar_tensor_tensor(out=flat(lg2), in0=flat(one1), scalar=-3.0e38, in1=flat(lg),
                                                            op0=ALU.mult, op1=ALU.add))
                step(nc.vector.tensor_tensor(gapv, m2, m1, ALU.subtract))
                dve.sem_inc(gap, 1)
                step(nc.vector.tensor_tensor(both_, one1, one2, ALU.add))
                dve.sem_inc(chosen, 1)
                dve.wait_ge(gap_exp, 1)
                step(nc.vector.tensor_scalar(den, gexp, 1.0, None, ALU.add))
                step(nc.vector.reciprocal(p1[:, :], den))
                step(nc.vector.tensor_tensor(p2[:, :], p1[:, :], gexp, ALU.mult))
                dve.wait_ge(counted, 1)
                step(nc.vector.tensor_copy(flat(ta), psC[1][:, 0:TILES * E]))
                a, b = ta, tb
                for d in doublings(TILES):
                    step(nc.vector.tensor_copy(b[:, 0:d, :], a[:, 0:d, :]))
                    step(nc.vector.tensor_tensor(b[:, d:, :], a[:, d:, :], a[:, 0:TILES - d, :], ALU.add))
                    a, b = b, a
                step(nc.vector.tensor_tensor(flat(exc), flat(a), psC[1][:, 0:TILES * E], ALU.subtract))
                step(nc.vector.tensor_scalar(te, a[:, TILES - 1, :], float(P - 1), None, ALU.add))
                step(nc.vector.tensor_copy(te_i, te))
                step(nc.vector.tensor_scalar(te_i, te_i, 7, None, ALU.arith_shift_right))
                step(nc.vector.tensor_copy(te, te_i))
                step(nc.vector.tensor_copy(tc, te))
                a, b = tc, td
                for d in doublings(E):
                    step(nc.vector.tensor_copy(b[:, 0:d], a[:, 0:d]))
                    step(nc.vector.tensor_tensor(b[:, d:], a[:, d:], a[:, 0:E - d], ALU.add))
                    a, b = b, a
                step(nc.vector.tensor_tensor(base, a, te, ALU.subtract))
                step(nc.vector.tensor_scalar(base, base, float(P), None, ALU.mult))
                step(nc.vector.tensor_tensor(flat(slot), flat(exc), psC[0][:, 0:TILES * E], ALU.add))
                step(nc.vector.tensor_tensor(slot, slot, by_expert(base), ALU.add))
                for k, one in enumerate((one1, one2)):
                    step(nc.vector.tensor_tensor(cand, one, slot, ALU.mult))
                    step(nc.vector.tensor_reduce(posf, cand, AX.X, ALU.add))
                    step(nc.vector.tensor_copy(pos[:, k, :], posf))
                step(nc.vector.tensor_scalar(den[:, 0:1], a[:, E - 1:E], -1.0, None, ALU.add))
                step(nc.vector.tensor_copy(nt_i[:, 0:1], den[:, 0:1]))
                step(nc.vector.tensor_scalar(nt_i[:, 1:2], nt_i[:, 0:1], 1, None, ALU.arith_shift_right))
                step(nc.vector.tensor_copy(ttab[0:1, 0:1], nt_i[0:1, 1:2]))
                step(nc.vector.tensor_scalar(trow[0:1, 0, :], iota[0:1, 0:SLOT_TILES], a[0:1, 0:1], None, ALU.is_ge))
                for e in range(1, E - 1):
                    step(nc.vector.scalar_tensor_tensor(
                        out=trow[0:1, e % 2, :], in0=iota[0:1, 0:SLOT_TILES], scalar=a[0:1, e:e + 1],
                        in1=trow[0:1, 1 - e % 2, :], op0=ALU.is_ge, op1=ALU.add))
                step(nc.vector.tensor_copy(ttab[0:1, 1:], trow[0:1, E % 2, :]))

            @block.tensor
            def _(pe):
                pe.sem_inc(x1_mm, 2)
                pe.sem_inc(xn3_read, 2)
                pe.sem_inc(gate_mm, 2)
                pe.wait_ge(m_in, 96)
                pe.wait_ge(masked, 1)
                for h in range(PAIRS):
                    last = nc.tensor.matmul(psA[h // 2][:, (h % 2) * D:(h % 2 + 1) * D], dots[:, h, :], wo[:, h, :],
                                            start=True, stop=True)
                last.then_inc(dwo_mm, 1)
                pe.wait_ge(dwo_ready, 1)
                for c in range(KD):
                    for h in range(PAIRS):
                        last = nc.tensor.matmul(psB[c][:, 0:D], wq[:, h, c * P:(c + 1) * P], dwo[:, h, :],
                                                start=(h == 0), stop=(h == PAIRS - 1))
                last.then_inc(m_mm, 1)
                pe.wait_ge(m_ready, 1)

                def product(c):
                    pe.wait_ge(xl_in[c.s], c.uses * 16 + 16)
                    pe.wait_ge(x1_add, c.t + 1)
                    for k in range(KD):
                        last = nc.tensor.matmul(psC[c.s][:, 0:D], xT[:, c.s, k, :], mtot[:, k, :],
                                                start=(k == 0), stop=(k == KD - 1))
                    last.then_inc(x1_mm, 1)
                over_tiles(pe, product)

                def turn(c):
                    pe.wait_ge(xn3_ready, c.t + 1)
                    pe.wait_ge(xT3_ready, c.t + 1)
                    for k in range(KD):
                        last = nc.tensor.transpose(psA[c.s][:, k * P:(k + 1) * P], xn[:, c.s, k * P:(k + 1) * P],
                                                   ident[:, :])
                    last.then_inc(xn3_read, 1)

                def gate(c):
                    pe.wait_ge(xT3_ready, c.t + 3)
                    for k in range(KD):
                        last = nc.tensor.matmul(psE[:, bass.ds(c.t * E, E)], xT[:, c.s, k, :], wg[:, k, :],
                                                start=(k == 0), stop=(k == KD - 1))
                    last.then_inc(gate_mm, 1)

                def both(c, b):
                    turn(c)
                    gate(b)
                over_tiles_lagged(pe, turn, both, gate)
                pe.wait_ge(chosen, 1)
                nc.tensor.matmul(psC[0][:, 0:TILES * E], before[:, :], flat(both_), start=True, stop=True)
                nc.tensor.matmul(psC[1][:, 0:TILES * E], ones[:, :], flat(both_), start=True, stop=True).then_inc(counted, 1)

        late = Arena(big)
        w1 = late.take(E * KD, H)
        w2 = late.take(E * HJ, D)
        ew_in = sem("ew_in")
        row_ready, row_free = sem("row_ready"), [sem(f"row_free{s}") for s in range(DEEP)]
        with nc.Block() as block:
            @block.sync
            def _(sp):
                for e in range(E):
                    sp.dma_start(w1[:, e * KD:(e + 1) * KD, :],
                                 w_1[e, :, :].rearrange("(k p) h -> p k h", p=P)).then_inc(ew_in, 16)
                    sp.dma_start(w2[:, e * HJ:(e + 1) * HJ, :],
                                 w_2[e, :, :].rearrange("(j p) d -> p j d", p=P)).then_inc(ew_in, 16)
                sp.wait_ge(ew_in, 16 * 2 * E)

            @block.vector
            def _(dve):
                def norm(c):
                    wait_apart(dve, (row_free[c.s], c.uses * (16 * TOPK)))
                    for k in range(TOPK):
                        nc.vector.tensor_copy(posx[:, c.s, k:k + 1], pos[:, k, bass.ds(c.t, 1)]).then_inc(row_ready, 1)
                    nc.vector.tensor_scalar(xn[:, c.s, :], acc[:, c.t, :], mean[:, bass.ds(c.t, 1)],
                                            rstd[:, bass.ds(c.t, 1)], ALU.subtract, ALU.mult).then_inc(row_ready, 1)
                over_tiles(dve, norm, DEEP)

            @block.gpsimd
            def _(pool):
                def scatter(c):
                    wait_apart(pool, (row_ready, c.t * 3 + 3))
                    for k in range(TOPK):
                        nc.gpsimd.indirect_dma_start(
                            out=xslot_d, out_offset=bass.IndirectOffsetOnAxis(ap=posx[:, c.s, k:k + 1], axis=0),
                            in_=xn[:, c.s, :], in_offset=None).then_inc(row_free[c.s], 16)
                over_tiles(pool, scatter, DEEP)
                for k in range(DEEP):
                    pool.wait_ge(row_free[k], 16 * TOPK * (TILES // DEEP + (k == 0)))

        work = Arena(accs)
        w1s = work.take(2, KD, H)
        hT = work.take(2, HJ, P)
        b2 = work.take(E, D)
        xs = work.take(2, D)
        xsT = work.take(2, KD, P)
        y = work.take(2, D)
        b2_in = sem("b2_in")
        xs_in = [sem(f"xs_in{s}") for s in range(2)]
        y_out = [sem(f"y_out{s}") for s in range(2)]
        xs_read, xsT_ready, w1s_ready, g1_done, hT_ready, g2_done, y_ready = (sem(n) for n in (
            "xs_read", "xsT_ready", "w1s_ready", "g1_done", "hT_ready", "g2_done", "y_ready"))
        hidden = (psB, [p[:, :] for p in psC])

        class Slots(Tile):
            pass

        def over_slots(eng, head, both, tail):
            m = eng.value_load(ttab[0:1, 0:1], min_val=LEAST_TILES // 2 - 1, max_val=SLOT_TILES // 2 - 1)
            head(Tile(0, 0, 0))
            both(Tile(1, 1, 0), Tile(0, 0, 0), True)
            both(Tile(2, 0, 1), Tile(1, 1, 0), True)
            with eng.Fori(1, m) as i:
                both(Tile(i * 2 + 1, 1, i), Tile(i * 2, 0, i), True)
                both(Tile(i * 2 + 2, 0, i + 1), Tile(i * 2 + 1, 1, i), True)
            both(Tile(m * 2 + 1, 1, m), Tile(m * 2, 0, m), False)
            tail(Tile(m * 2 + 1, 1, m))

        with nc.Block() as block:
            @block.sync
            def _(sp):
                sp.dma_start(b2, b_2.partition_broadcast(P)).then_inc(b2_in, 16)
                xr = xslot_d.rearrange("(t p) d -> t p d", p=P)

                def load(t, s):
                    sp.dma_start(xs[:, s, :], xr[bass.ds(t, 1), :, :].rearrange("a p d -> (a p) d")).then_inc(xs_in[s], 16)

                def head(c):
                    load(0, 0)
                    load(1, 1)

                def both(c, b, more):
                    if more:
                        sp.wait_ge(xs_read, c.t)
                        load(c.t + 1, b.s)
                over_slots(sp, head, both, lambda c: None)

            @block.gpsimd
            def _(pool):
                yr = yslot_d.rearrange("(t p) d -> t p d", p=P)

                def store(b):
                    wait_apart(pool, (y_ready, b.t + 3))
                    pool.dma_start(yr[bass.ds(b.t, 1), :, :].rearrange("a p d -> (a p) d"), y[:, b.s, :]).then_inc(y_out[b.s], 16)

                def tail(c):
                    store(c)
                    wait_apart(pool,
                               (y_out[0], c.uses * 16 + 16),
                               (y_out[1], c.uses * 16 + 16))
                over_slots(pool, lambda c: None, lambda c, b, more: store(b), tail)

            @block.scalar
            def _(act):
                act.sem_inc(xsT_ready, 2)
                act.sem_inc(hT_ready, 2 * HJ)

                def take_xs(t, s):
                    wait_apart(act,
                               (xs_read, t + 1),
                               (g1_done, t + 1))
                    nc.scalar.activation(flat(xsT[:, s, :, :]), psA[0][:, 0:D], ACT.Copy).then_inc(xsT_ready, 1)

                def relu(c):
                    e = act.value_load(ttab[0:1, bass.ds(c.t + 1, 1)], min_val=0, max_val=E - 1)
                    wait_apart(act,
                               (g1_done, c.t + 3),
                               (g2_done, c.t + 1))
                    for j in range(HJ):
                        nc.scalar.activation(hT[:, c.s, j, :], hidden[c.s][j // 4][:, (j % 4) * P:(j % 4 + 1) * P],
                                             ACT.Relu, bias=b1T[:, bass.ds(e * HJ + j, 1)]).then_inc(hT_ready, 1)

                def head(c):
                    take_xs(0, 0)
                    take_xs(1, 1)
                    relu(c)

                def both(c, b, more):
                    if more:
                        take_xs(c.t + 1, b.s)
                    relu(c)
                over_slots(act, head, both, lambda c: None)

            @block.vector
            def _(dve):
                dve.sem_inc(y_ready, 2)
                dve.wait_ge(b2_in, 16)

                def take_w1(t, s):
                    e = dve.value_load(ttab[0:1, bass.ds(t + 1, 1)], min_val=0, max_val=E - 1)
                    wait_apart(dve, (g1_done, t + 1))
                    nc.vector.tensor_copy(w1s[:, s, :, :], w1[:, bass.ds(e * KD, KD), :]).then_inc(w1s_ready, 1)

                def take_y(b):
                    e = dve.value_load(ttab[0:1, bass.ds(b.t + 1, 1)], min_val=0, max_val=E - 1)
                    dve.wait_ge(g2_done, b.t + 3)
                    wait(dve, y_out[b.s], b.uses * 16)
                    nc.vector.tensor_tensor(y[:, b.s, :], (psD, psE)[b.s][:, 0:D], b2[:, e, :], ALU.add).then_inc(y_ready, 1)

                def head(c):
                    take_w1(0, 0)
                    take_w1(1, 1)

                def both(c, b, more):
                    if more:
                        take_w1(c.t + 1, b.s)
                    take_y(b)
                over_slots(dve, head, both, take_y)

            @block.tensor
            def _(pe):
                pe.sem_inc(g1_done, 2)
                pe.sem_inc(g2_done, 2)

                def turn_x(t, s, uses):
                    pe.wait_ge(xs_in[s], uses * 16 + 16)
                    pe.wait_ge(xsT_ready, t + 2)
                    for k in range(KD):
                        last = nc.tensor.transpose(psA[0][:, k * P:(k + 1) * P], xs[:, s, k * P:(k + 1) * P], ident[:, :])
                    last.then_inc(xs_read, 1)

                def first(c):
                    pe.wait_ge(w1s_ready, c.t + 1)
                    pe.wait_ge(xsT_ready, c.t + 3)
                    pe.wait_ge(hT_ready, c.t * HJ + HJ)
                    for j in range(HJ):
                        for k in range(KD):
                            last = nc.tensor.matmul(hidden[c.s][j // 4][:, (j % 4) * P:(j % 4 + 1) * P],
                                                    w1s[:, c.s, k, j * P:(j + 1) * P], xsT[:, c.s, k, :],
                                                    start=(k == 0), stop=(k == KD - 1))
                    last.then_inc(g1_done, 1)

                def second(b):
                    e = pe.value_load(ttab[0:1, bass.ds(b.t + 1, 1)], min_val=0, max_val=E - 1)
                    pe.wait_ge(hT_ready, b.t * HJ + 3 * HJ)
                    pe.wait_ge(y_ready, b.t + 1)
                    for j in range(HJ):
                        last = nc.tensor.matmul((psD, psE)[b.s][:, 0:D], hT[:, b.s, j, :], w2[:, e * HJ + j, :],
                                                start=(j == 0), stop=(j == HJ - 1))
                    last.then_inc(g2_done, 1)

                def head(c):
                    turn_x(0, 0, 0)
                    turn_x(1, 1, 0)
                    first(c)

                def both(c, b, more):
                    if more:
                        turn_x(c.t + 1, b.s, b.uses + 1)
                    first(c)
                    second(b)
                over_slots(pe, head, both, second)

        last_ = Arena(accs)
        x1r = last_.take(DEEP, D)
        yk = last_.take(DEEP * TOPK, D)
        osum = last_.take(DEEP, D)
        x1_in = [sem(f"x1_in{s}") for s in range(DEEP)]
        y_in = [sem(f"y_in{s}") for s in range(DEEP)]
        o_out = [sem(f"o_out{s}") for s in range(DEEP)]
        pos_ready, o_half, o_ready = sem("pos_ready"), sem("o_half"), sem("o_ready")
        with nc.Block() as block:
            @block.sync
            def _(sp):
                def head(c):
                    sp.dma_start(x1r[:, c.s, :], x1_d[bass.ds(c.t * P, P), :]).then_inc(x1_in[c.s], 16)

                def store(b):
                    sp.wait_ge(o_ready, b.t + 1 + DEEP)
                    sp.dma_start(out[bass.ds(b.t * P, P), :], osum[:, b.s, :]).then_inc(o_out[b.s], 16)

                def both(c, b):
                    sp.wait_ge(o_ready, c.t + 1)
                    head(c)
                    store(b)
                over_tiles_lagged(sp, head, both, store, DEEP)
                all_stored(sp, o_out)

            @block.gpsimd
            def _(pool):
                def gather(c):
                    wait_apart(pool, (o_ready, c.t + 1))
                    for k in range(TOPK):
                        nc.gpsimd.tensor_copy(posx[:, c.s, k:k + 1], pos[:, k, bass.ds(c.t, 1)]).then_inc(pos_ready, 1)
                    wait_apart(pool, (pos_ready, c.t * 2 + 2))
                    for k in range(TOPK):
                        nc.gpsimd.indirect_dma_start(
                            out=yk[:, c.s * TOPK + k, :], out_offset=None, in_=yslot_d,
                            in_offset=bass.IndirectOffsetOnAxis(ap=posx[:, c.s, k:k + 1], axis=0),
                        ).then_inc(y_in[c.s], 16)
                over_tiles(pool, gather, DEEP)

            @block.vector
            def _(dve):
                dve.sem_inc(o_ready, DEEP)

                def combine(c):
                    dve.wait_ge(x1_in[c.s], c.uses * 16 + 16)
                    dve.wait_ge(y_in[c.s], c.uses * 32 + 32)
                    wait(dve, o_out[c.s], c.uses * 16)
                    nc.vector.scalar_tensor_tensor(
                        out=osum[:, c.s, :], in0=yk[:, c.s * TOPK, :], scalar=p1[:, bass.ds(c.t, 1)],
                        in1=x1r[:, c.s, :], op0=ALU.mult, op1=ALU.add).then_inc(o_half, 1)
                    dve.wait_ge(o_half, c.t + 1)
                    nc.vector.scalar_tensor_tensor(
                        out=osum[:, c.s, :], in0=yk[:, c.s * TOPK + 1, :], scalar=p2[:, bass.ds(c.t, 1)],
                        in1=osum[:, c.s, :], op0=ALU.mult, op1=ALU.add).then_inc(o_ready, 1)
                over_tiles(dve, combine, DEEP)


def kernel(**a):
    import concourse.bacc as bacc
    from concourse.bass_utils import run_bass_kernel_spmd

    def np_(name):
        return np.ascontiguousarray(np.asarray(a[name]))

    def padded(v, n, value=0):
        return np.concatenate([v, np.full((n - len(v), *v.shape[1:]), value, v.dtype)])

    def edge_cols(v):
        return np.ascontiguousarray(v.reshape(ECOLS, P).T)

    wqkv = np_("L0_mix_w_qkv")
    arrays = {
        "x": padded(np_("x"), ROWS),
        "src": edge_cols(padded(np_("src"), ECOLS * P)),
        "dst": edge_cols(padded(np_("dst"), ECOLS * P, NODES - 1)),
        "ew": edge_cols(padded(np_("edge_weight"), ECOLS * P)),
        "w_self": np_("L0_gnn_W_self"),
        "w_nb": np_("L0_gnn_W_neighbor"),
        "gnn_bias": np_("L0_gnn_bias"),
        "w_q": np.ascontiguousarray(wqkv[:INNER]),
        "w_kv": np.ascontiguousarray(wqkv[INNER:].T),
        "w_o": np.ascontiguousarray(np_("L0_mix_w_out").T),
        "b_out": np_("L0_mix_b_out"),
        "w_g": np.ascontiguousarray(np_("L0_ffn_Wg").T),
        "b_g": np_("L0_ffn_bg"),
        "w_1": np.ascontiguousarray(np_("L0_ffn_W1").transpose(0, 2, 1)),
        "b_1": np.ascontiguousarray(np_("L0_ffn_b1").reshape(E * HJ, P).T),
        "w_2": np.ascontiguousarray(np_("L0_ffn_W2").transpose(0, 2, 1)),
        "b_2": np_("L0_ffn_b2"),
    }
    nc = bacc.Bacc("TRN2", target_bir_lowering=False, num_devices=1)
    args = [nc.dram_tensor(n, v.shape, mybir.dt.from_np(v.dtype), kind="ExternalInput").ap() for n, v in arrays.items()]
    out = nc.dram_tensor("out", (ROWS, D), F32, kind="ExternalOutput").ap()
    graph_layer(nc, *args, out)
    r = run_bass_kernel_spmd(nc, [arrays], core_ids=[0])
    return r.results[0]["out"][:NODES]
```
